# Optimizing a Trainium2 kernel written in Bass

```python
import numpy as np
import jax
import jax.numpy as jnp

def _softmax(x, axis=-1):
    return jax.nn.softmax(x, axis=axis)

def _gelu(x):
    return jax.nn.gelu(x, approximate=True)

def _silu(x):
    return jax.nn.silu(x)

def _sigmoid(x):
    return jax.nn.sigmoid(x)

def _layernorm(x, axis=-1, eps=1e-05):
    m = jnp.mean(x, axis=axis, keepdims=True)
    v = jnp.var(x, axis=axis, keepdims=True)
    return (x - m) / jnp.sqrt(v + eps)

def _scatter_add(tgt, idx, src, axis=0):
    return tgt.at[idx].add(src)

def _segment_sum(src, seg, n):
    return jax.ops.segment_sum(src, seg, n)
kernel_name = 'mk_recurrent_d1_jaxref_r4_c4e8fe'

def setup_inputs(seed: int=0):
    np.random.seed(seed)
    _w = jnp.asarray

    def _L0_attn_setup():
        import jax, jax.numpy as jnp
        import numpy as np
        B, N, E = (4, 1024, 512)
        H_DIM = 512
        HEADS = 16
        DH = H_DIM // HEADS
        LN_EPS = 1e-05

        def _heads(t):
            b, n, _ = t.shape
            return t.reshape(b, n, HEADS, DH).transpose(0, 2, 1, 3)

        def _layernorm(x, g, b):
            mu = jnp.mean(x, axis=-1, keepdims=True)
            var = jnp.mean(jnp.square(x - mu), axis=-1, keepdims=True)
            return (x - mu) * jax.lax.rsqrt(var + LN_EPS) * g + b
        key = jax.random.key(seed)
        ks = jax.random.split(key, 10)
        s = 1.0 / np.sqrt(E)
        so = 1.0 / np.sqrt(H_DIM)
        return {'x': jax.random.normal(ks[0], (B, N, E), jnp.float32), 'Wqk': jax.random.normal(ks[1], (E, H_DIM), jnp.float32) * s, 'bqk': jnp.zeros((H_DIM,), jnp.float32), 'Wv': jax.random.normal(ks[2], (E, H_DIM), jnp.float32) * s, 'bv': jnp.zeros((H_DIM,), jnp.float32), 'Wu': jax.random.normal(ks[3], (E, H_DIM), jnp.float32) * s, 'bu': jnp.zeros((H_DIM,), jnp.float32), 'Wo': jax.random.normal(ks[4], (H_DIM, E), jnp.float32) * so, 'bo': jnp.zeros((E,), jnp.float32), 'ln_g': jnp.ones((H_DIM,), jnp.float32), 'ln_b': jnp.zeros((H_DIM,), jnp.float32)}
    _L0_attn_in = _L0_attn_setup()

    def _L0_ffn_setup():
        import jax, jax.numpy as jnp
        import numpy as np
        DIM_IN = 512
        DIM_HIDDEN = 2048
        key = jax.random.key(seed)
        k_x, k_g, k_u, k_d = jax.random.split(key, 4)
        s_in = 1.0 / np.sqrt(DIM_IN)
        s_hid = 1.0 / np.sqrt(DIM_HIDDEN)
        x = jax.random.normal(k_x, (4, 512, DIM_IN), dtype=jnp.float32)
        w_gate = jax.random.uniform(k_g, (DIM_HIDDEN, DIM_IN), jnp.float32, -s_in, s_in)
        w_up = jax.random.uniform(k_u, (DIM_HIDDEN, DIM_IN), jnp.float32, -s_in, s_in)
        w_down = jax.random.uniform(k_d, (DIM_IN, DIM_HIDDEN), jnp.float32, -s_hid, s_hid)
        return {'x': x, 'w_gate': w_gate, 'w_up': w_up, 'w_down': w_down}
    _L0_ffn_in = _L0_ffn_setup()
    _d = {'L0_attn_x': _L0_attn_in['x'], 'L0_attn_Wqk': _L0_attn_in['Wqk'], 'L0_attn_bqk': _L0_attn_in['bqk'], 'L0_attn_Wv': _L0_attn_in['Wv'], 'L0_attn_bv': _L0_attn_in['bv'], 'L0_attn_Wu': _L0_attn_in['Wu'], 'L0_attn_bu': _L0_attn_in['bu'], 'L0_attn_Wo': _L0_attn_in['Wo'], 'L0_attn_bo': _L0_attn_in['bo'], 'L0_attn_ln_g': _L0_attn_in['ln_g'], 'L0_attn_ln_b': _L0_attn_in['ln_b'], 'L0_ffn_w_gate': _L0_ffn_in['w_gate'], 'L0_ffn_w_up': _L0_ffn_in['w_up'], 'L0_ffn_w_down': _L0_ffn_in['w_down']}
    _x0 = _d['L0_attn_x']
    _d['L0_attn_x'] = jax.random.normal(jax.random.fold_in(jax.random.key(seed), 1), (1, 2048, 512), dtype=_x0.dtype)
    del _x0
    return _d

def reference(L0_attn_x, L0_attn_Wqk, L0_attn_bqk, L0_attn_Wv, L0_attn_bv, L0_attn_Wu, L0_attn_bu, L0_attn_Wo, L0_attn_bo, L0_attn_ln_g, L0_attn_ln_b, L0_ffn_w_gate, L0_ffn_w_up, L0_ffn_w_down):

    def _L0_attn_ref(x, Wqk, bqk, Wv, bv, Wu, bu, Wo, bo, ln_g, ln_b):
        import jax, jax.numpy as jnp
        import numpy as np
        B, N, E = (4, 1024, 512)
        H_DIM = 512
        HEADS = 16
        DH = H_DIM // HEADS
        LN_EPS = 1e-05

        def _heads(t):
            b, n, _ = t.shape
            return t.reshape(b, n, HEADS, DH).transpose(0, 2, 1, 3)

        def _layernorm(x, g, b):
            mu = jnp.mean(x, axis=-1, keepdims=True)
            var = jnp.mean(jnp.square(x - mu), axis=-1, keepdims=True)
            return (x - mu) * jax.lax.rsqrt(var + LN_EPS) * g + b
        q = x @ Wqk + bqk
        k = x @ Wqk + bqk
        v = jax.nn.silu(x @ Wv + bv)
        u = jax.nn.silu(x @ Wu + bu)
        q = jax.nn.elu(_heads(q))
        kh = jax.nn.elu(_heads(k))
        vh = _heads(v)
        kv = jnp.einsum('bhnd,bhne->bhde', kh, vh)
        out = jnp.einsum('bhnd,bhde->bhne', q, kv)
        out = out.transpose(0, 2, 1, 3).reshape(x.shape[0], x.shape[1], H_DIM)
        out = _layernorm(out, ln_g, ln_b)
        out = u * out
        return out @ Wo + bo

    def _L0_ffn_ref(x, w_gate, w_up, w_down):
        import jax, jax.numpy as jnp
        import numpy as np
        DIM_IN = 512
        DIM_HIDDEN = 2048
        gate = jnp.einsum('bsd,hd->bsh', x, w_gate)
        up = jnp.einsum('bsd,hd->bsh', x, w_up)
        gated = jax.nn.silu(gate) * up
        return jnp.einsum('bsh,dh->bsd', gated, w_down)
    x = L0_attn_x
    xn = _layernorm(x, axis=-1)
    s = _L0_attn_ref(xn, L0_attn_Wqk, L0_attn_bqk, L0_attn_Wv, L0_attn_bv, L0_attn_Wu, L0_attn_bu, L0_attn_Wo, L0_attn_bo, L0_attn_ln_g, L0_attn_ln_b)
    g = _silu(_L0_ffn_ref(xn, L0_ffn_w_gate, L0_ffn_w_up, L0_ffn_w_down))
    x = x + s * g
    return x

_drawn_inputs = setup_inputs


def setup_inputs(seed=0):
    import zlib

    import numpy as np

    out = dict(_drawn_inputs(seed))
    spreads = {'L0_attn_bqk': (0.0, 0.458),
     'L0_attn_bv': (0.0, 0.569),
     'L0_attn_bu': (0.0, 0.8),
     'L0_attn_bo': (0.0, 0.8),
     'L0_attn_ln_g': (1.0, 0.6),
     'L0_attn_ln_b': (0.0, 0.8)}
    factors = {}
    for name, (base, spread) in spreads.items():
        noise = np.random.default_rng([zlib.crc32(name.encode()), seed]).standard_normal(out[name].shape)
        drawn = base * np.exp(spread * noise) if base else spread * noise
        out[name] = jnp.asarray(drawn.astype(out[name].dtype))
    for name, factor in factors.items():
        out[name] = (out[name] * factor).astype(out[name].dtype)
    return out
```

```python
from contextlib import ExitStack

import numpy as np

import concourse.bass as bass
from concourse import mybir
from concourse.alu_op_type import AluOpType as ALU

ACT = mybir.ActivationFunctionType
F32 = mybir.dt.float32
F32R = mybir.dt.float32r

P = 128
TILE = 512
EPS = 1e-5
DH = 32


def build(nc, x, xT, wqk, wv, wu, wo, wg, wup, wd, bqk, bu, bo, ln_g, ln_b, bv, outT):
    N, D = x.shape
    NT = N // TILE
    NB = TILE // P
    NK = D // P
    NC = wg.shape[0]
    assert D == TILE and NT == 4 and NB == 4 and NK == 4 and NC % 2 == 0
    W_UNITS = 4 * NK
    C_UNITS = 3
    HALF = P // DH

    ctx = ExitStack()
    with ctx:
        def sb(name, shape, dt=F32):
            return ctx.enter_context(nc.sbuf_tensor(name, shape, dt))

        def sem(name):
            return ctx.enter_context(nc.semaphore(name))

        xn_hi = sb("xn_hi", [P, NK, N], F32R)
        xn_lo = sb("xn_lo", [P, NK, N], F32R)
        kf = sb("kf", [P, NK, N])
        st = sb("st", [P, NK, N])
        region_hi = [sb(f"region{r}_hi", [P, NK, TILE], F32R) for r in range(2)]
        region_lo = [sb(f"region{r}_lo", [P, NK, TILE], F32R) for r in range(2)]
        stage = sb("stage", [P, NK, TILE])
        cur_hi = sb("cur_hi", [P, NK, TILE], F32R)
        cur_lo = sb("cur_lo", [P, NK, TILE], F32R)
        kcur = sb("kcur", [P, NK, TILE])
        nat = sb("nat", [P, NB, TILE])
        tmp = sb("tmp", [P, 2, TILE])
        kvblk = sb("kvblk", [P, NK, P])
        cols = sb("cols", [P, 5, NK])
        ident = sb("ident", [P, P])
        stats = sb("stats", [P, NB, 6])
        mean, mean_sum, mean_dif, dev_sum, var_in, var_out = (
            sb(name, [P, NB]) for name in ("mean", "mean_sum", "mean_dif", "dev_sum", "var_in", "var_out"))
        veps = sb("veps", [P, NB])
        rstd = sb("rstd", [P, NB])
        half = sb("half", [P, NB])
        k_nat = st[:, :, 0:TILE]
        v_nat = st[:, :, TILE:2 * TILE]
        bv_all = st[:, 0, 2 * TILE:3 * TILE]
        BQK, BU, BO, LNG, LNB = range(5)
        bank = [ctx.enter_context(nc.psum_tensor(f"bank{b}", [P, TILE], F32)) for b in range(8)]

        consts_loaded = sem("consts_loaded")
        x_loaded = [sem(f"x_loaded{b}") for b in range(NB)]
        w_loaded = [sem(f"w_loaded{k}") for k in range(NK)]
        xt_loaded = sem("xt_loaded")
        out_stored = [sem(f"out_stored{m}") for m in range(NK)]
        ident_zeroed = sem("ident_zeroed")
        ident_ready = sem("ident_ready")
        half_ready = sem("half_ready")
        w_hi = sem("w_hi")
        w_split = sem("w_split")
        ln_stats = sem("ln_stats")
        ln_halves = sem("ln_halves")
        ln_terms = sem("ln_terms")
        ln_veps = sem("ln_veps")
        ln_rstd = sem("ln_rstd")
        nat_ready = sem("nat_ready")
        xt_ready = sem("xt_ready")
        x_hi = sem("x_hi")
        x_split = sem("x_split")
        xn_kept = sem("xn_kept")
        kt_ready = sem("kt_ready")
        exp_done = sem("exp_done")
        expm1_done = sem("expm1_done")
        kt_done = sem("kt_done")
        v_ready = sem("v_ready")
        v_biased = sem("v_biased")
        v_done = sem("v_done")
        knat_ready = sem("knat_ready")
        knat_done = sem("knat_done")
        kv_ready = sem("kv_ready")
        kv_added = sem("kv_added")
        k_kept = sem("k_kept")
        k_back = sem("k_back")
        f_zeroed = sem("f_zeroed")
        ut_ready = sem("ut_ready")
        ut_done = sem("ut_done")
        o_ready = sem("o_ready")
        zt_ready = sem("zt_ready")
        zg_done = sem("zg_done")
        y_done = sem("y_done")
        y_hi = sem("y_hi")
        y_split = sem("y_split")
        s_ready = sem("s_ready")
        s_done = sem("s_done")
        gate_ready = sem("gate_ready")
        up_ready = sem("up_ready")
        gate_done = sem("gate_done")
        h_done = sem("h_done")
        h_hi = sem("h_hi")
        h_split = sem("h_split")
        f_ready = sem("f_ready")
        sums_taken = sem("sums_taken")
        g_done = sem("g_done")
        sg_done = sem("sg_done")
        out_done = sem("out_done")

        block = ctx.enter_context(nc.Block())

        def f32(ap):
            return ap.bitcast(F32)

        def wait_alone(eng, semaphore, value):
            eng.wait_ge(ident_ready, 1)
            eng.wait_ge(semaphore, value)

        def cols_of(t):
            return bass.ds(t * TILE, TILE)

        def chunk_units(c):
            return W_UNITS + C_UNITS * c

        @block.sync
        def _(sp):
            def load_x(t, block_of_tile):
                sp.dma_start(nat[:, block_of_tile, :], x[bass.ds(t * TILE + block_of_tile * P, P), :])\
                  .then_inc(x_loaded[block_of_tile], 16)

            def load_w(dram, k):
                sp.dma_start(stage[:, k, :], dram[k, :, :]).then_inc(w_loaded[k], 16)

            def load_chunk(c):
                for u, dram in enumerate((wg, wup, wd)):
                    sp.wait_ge(w_split, chunk_units(c) - C_UNITS + u + 1)
                    sp.dma_start(stage[:, u, :], dram[bass.ds(c, 1), :, :].rearrange("a p n -> p (a n)"))\
                      .then_inc(w_loaded[u], 16)

            for k in range(NK):
                load_x(0, k)
                load_w(wqk, k)
            for j, (dst, src) in enumerate(((cols[:, BQK, :], bqk), (cols[:, BU, :], bu), (cols[:, BO, :], bo),
                                            (cols[:, LNG, :], ln_g), (cols[:, LNB, :], ln_b),
                                            (bv_all, bv.partition_broadcast(P)))):
                sp.dma_start(dst, src).then_inc(consts_loaded, 16)
            for k in range(NK):
                sp.wait_ge(w_split, k + 1)
                load_w(wv, k)
            with sp.Fori(0, NT - 1) as t:
                sp.wait_ge(xt_ready, NB * (t + 1))
                for b in range(NB):
                    load_x(t + 1, b)
            for j, dram in ((2, wu), (3, wo)):
                for k in range(NK):
                    sp.wait_ge(w_split, NK * (j - 1) + k + 1)
                    load_w(dram, k)
            for u, dram in enumerate((wg, wup, wd)):
                sp.wait_ge(w_split, W_UNITS - NK + u + 1)
                sp.dma_start(stage[:, u, :], dram[0, :, :]).then_inc(w_loaded[u], 16)
            with sp.Fori(1, NC) as c:
                load_chunk(c)
            sp.wait_ge(s_ready, NK * NT)
            sp.dma_start(kcur[:, :, :], xT[:, :, 0:TILE]).then_inc(xt_loaded, 16)
            for t in range(NT):
                for m in range(NK):
                    sp.wait_ge(out_done, NK * t + m + 1)
                    sp.dma_start(outT[:, m, t * TILE:(t + 1) * TILE], nat[:, m, :]).then_inc(out_stored[m], 16)
                if t + 1 < NT:
                    sp.dma_start(kcur[:, :, :], xT[:, :, (t + 1) * TILE:(t + 2) * TILE]).then_inc(xt_loaded, 16)
            for m in range(NK):
                sp.wait_ge(out_stored[m], 16 * NT)

        @block.gpsimd
        def _(pool):
            def power(n):
                pool.wait_ge(ln_veps, n + 1)
                pool.tensor_tensor(rstd[:, :], veps[:, :], half[:, :], ALU.pow).then_inc(ln_rstd, 1)

            def keep_xn(t):
                pool.wait_ge(x_split, NB * (t + 1))
                pool.tensor_copy(xn_hi[:, :, cols_of(t)], f32(cur_hi[:, :, :])).then_inc(xn_kept, 1)
                pool.tensor_copy(xn_lo[:, :, cols_of(t)], f32(cur_lo[:, :, :])).then_inc(xn_kept, 1)

            pool.memset(half[:, :], -0.5).then_inc(half_ready, 1)
            pool.memset(ident[:, :], 0.0).then_inc(ident_zeroed, 1)
            pool.wait_ge(ident_zeroed, 1)
            pool.affine_select(out=ident[:, :], in_=ident[:, :], compare_op=ALU.not_equal, fill=1.0,
                               base=0, pattern=[[-1, P]], channel_multiplier=1).then_inc(ident_ready, 1)
            pool.wait_ge(half_ready, 1)
            power(0)
            with pool.Fori(0, NT - 1) as t:
                keep_xn(t)
                pool.wait_ge(kt_done, NK * (t + 1))
                pool.tensor_copy(kf[:, :, cols_of(t)], kcur[:, :, :]).then_inc(k_kept, 1)
                power(t + 1)
            keep_xn(NT - 1)

            def b_step(s, more):
                power(s + NT)
                if more:
                    pool.wait_ge(o_ready, NB * (s + 1))
                    pool.wait_ge(k_kept, NT - 1)
                    pool.tensor_copy(kcur[:, :, :], kf[:, :, cols_of(s)]).then_inc(k_back, 1)

            with pool.Fori(0, NT - 1) as s:
                b_step(s, True)
            pool.wait_ge(k_back, NT - 1)
            pool.memset(kf[:, :, :], 0.0).then_inc(f_zeroed, 1)
            b_step(NT - 1, False)

            for t in range(NT):
                pool.wait_ge(xt_loaded, 16 * (t + 1))
                for m in range(NK):
                    pool.wait_ge(sg_done, NK * t + m + 1)
                    pool.tensor_tensor(nat[:, m, :], nat[:, m, :], kcur[:, m, :], ALU.add).then_inc(out_done, 1)

        @block.scalar
        def _(act):
            def split_hi(unit, slot, dst, loaded):
                act.wait_ge(w_loaded[slot], loaded)
                act.activation(dst, stage[:, slot, :], ACT.Copy).then_inc(w_hi, 1)

            def split_matrix(j):
                for k in range(NK):
                    split_hi(NK * j + k, k, region_hi[j % 2][:, k, :], 16 * (j + 1))

            def split_chunk_unit(c, r, u):
                split_hi(chunk_units(c) + u, u, region_hi[r][:, u, :], 16 * (c + 5))

            def x_his(t):
                for b in range(NB):
                    act.wait_ge(xt_ready, NB * t + b + 1)
                    if not (isinstance(t, int) and t == 0) and b == 0:
                        act.wait_ge(xn_kept, 2 * t)
                    act.activation(cur_hi[:, :, b * P:(b + 1) * P],
                                   bank[b][:, :].rearrange("p (k n) -> p k n", k=NK), ACT.Copy).then_inc(x_hi, 1)

            def exps(t):
                for m in range(NK):
                    act.wait_ge(kt_ready, NK * t + m + 1)
                    if m >= 2:
                        act.wait_ge(kt_done, NK * t + m - 1)
                    act.activation(tmp[:, m % 2, :], bank[m][:, :], ACT.Exp, bias=cols[:, BQK, m:m + 1])\
                       .then_inc(exp_done, 1)

            def v_silus(t):
                for b in range(NB):
                    act.wait_ge(v_biased, NB * t + b + 1)
                    act.activation(v_nat[:, b, :], v_nat[:, b, :], ACT.Silu).then_inc(v_done, 1)

            def k_nats(t, banks):
                for b in range(NB):
                    act.wait_ge(knat_ready, NB * t + b + 1)
                    act.activation(k_nat[:, b, :], bank[banks[b]][:, :], ACT.Copy).then_inc(knat_done, 1)

            split_matrix(0)
            x_his(0)
            act.wait_ge(consts_loaded, 16 * 6)
            split_matrix(1)
            with act.Fori(0, NT - 1) as t:
                exps(t)
                v_silus(t)
                x_his(t + 1)
                k_nats(t, K_NAT_BANKS)
            exps(NT - 1)
            split_matrix(2)
            v_silus(NT - 1)
            split_matrix(3)
            k_nats(NT - 1, K_NAT_BANKS)

            def u_silus(s):
                for m in range(NK):
                    wait_alone(act, ut_ready, NK * s + m + 1)
                    act.activation(st[:, m, cols_of(s)], bank[m][:, :], ACT.Silu, bias=cols[:, BU, m:m + 1])\
                       .then_inc(ut_done, 1)

            def s_biases(s, done):
                for m in range(NK):
                    wait_alone(act, s_ready, NK * s + m + 1)
                    act.activation(st[:, m, cols_of(s)], bank[4 + m][:, :], ACT.Identity,
                                   bias=cols[:, BO, m:m + 1]).then_inc(done, 1)

            def y_hi_part(s, m):
                wait_alone(act, y_done, NK * s + m + 1)
                act.activation(cur_hi[:, m, :], st[:, m, cols_of(s)], ACT.Copy).then_inc(y_hi, 1)

            def zg_and_y_hi(s):
                for m in range(NK):
                    act.wait_ge(zt_ready, NK * s + m + 1)
                    act.activation(tmp[:, m % 2, :], bank[4 + m][:, :], ACT.Identity,
                                   bias=cols[:, LNB, m:m + 1], scale=cols[:, LNG, m:m + 1]).then_inc(zg_done, 1)
                    if m >= 1:
                        y_hi_part(s, m - 1)
                y_hi_part(s, NK - 1)

            u_silus(0)
            act.wait_ge(xn_kept, 2 * NT)
            zg_and_y_hi(0)
            with act.Fori(1, NT - 1) as s:
                u_silus(s)
                s_biases(s - 1, s_done)
                zg_and_y_hi(s)
            u_silus(NT - 1)
            for u in range(C_UNITS):
                split_chunk_unit(0, 0, u)
            s_biases(NT - 2, s_done)
            zg_and_y_hi(NT - 1)

            def gate_silu(n, t):
                act.wait_ge(gate_ready, n + 1)
                act.activation(tmp[:, t % 2, :], bank[2 * (t % 2)][:, :], ACT.Silu).then_inc(gate_done, 1)

            def h_hi_part(n, t):
                act.wait_ge(h_done, n + 1)
                act.activation(cur_hi[:, t % 2, :], tmp[:, t % 2, :], ACT.Copy).then_inc(h_hi, 1)

            def c_chunk(c, r):
                last = isinstance(c, int) and c == NC - 1
                for t in range(NT):
                    n, nt = NT * c + t, (t + 1) % NT
                    if not (last and t == NT - 1):
                        gate_silu(n + 1, nt)
                        h_hi_part(n + 1, nt)
                    if not last and t < C_UNITS:
                        split_chunk_unit(c + 1, 1 - r, t)
                    if last:
                        for m in range(NK):
                            act.wait_ge(sums_taken, NK * (n + 1) + m + 1)
                            if t:
                                act.wait_ge(out_stored[m], 16 * t)
                            act.activation(nat[:, m, :], kf[:, m, cols_of(t)], ACT.Silu).then_inc(g_done, 1)

            gate_silu(0, 0)
            act.wait_ge(s_ready, NK * NT)
            h_hi_part(0, 0)
            s_biases(NT - 1, sums_taken)
            with act.Fori(0, NC - 2, 2) as c:
                c_chunk(c, 0)
                c_chunk(c + 1, 1)
            c_chunk(NC - 2, 0)
            c_chunk(NC - 1, 1)

        @block.vector
        def _(dve):
            def split_lo(unit, slot, hi, lo):
                dve.wait_ge(w_hi, unit + 1)
                dve.tensor_tensor(lo, stage[:, slot, :], f32(hi), ALU.subtract).then_inc(w_split, 1)

            def split_matrix(j):
                for k in range(NK):
                    split_lo(NK * j + k, k, region_hi[j % 2][:, k, :], region_lo[j % 2][:, k, :])

            def split_chunk_unit(c, r, u):
                split_lo(chunk_units(c) + u, u, region_hi[r][:, u, :], region_lo[r][:, u, :])

            def layernorm(n, source, arrived):
                for b in range(NB):
                    arrived(b)
                    dve.bn_stats(stats[:, b, :], source(b)).then_inc(ln_stats, 1)
                mean_e, dev_e, mean_o, dev_o = (stats[:, :, i] for i in (1, 2, 4, 5))
                dve.wait_ge(ln_stats, NB * (n + 1))
                dve.tensor_tensor(mean_sum[:, :], mean_e, mean_o, ALU.add).then_inc(ln_halves, 1)
                dve.tensor_tensor(mean_dif[:, :], mean_e, mean_o, ALU.subtract).then_inc(ln_halves, 1)
                dve.tensor_tensor(dev_sum[:, :], dev_e, dev_o, ALU.add).then_inc(ln_halves, 1)
                dve.wait_ge(ln_halves, 3 * (n + 1))
                dve.tensor_scalar(mean[:, :], mean_sum[:, :], 0.5, None, ALU.mult).then_inc(ln_terms, 1)
                dve.tensor_scalar(var_in[:, :], dev_sum[:, :], 1.0 / D, EPS, ALU.mult, ALU.add).then_inc(ln_terms, 1)
                dve.scalar_tensor_tensor(out=var_out[:, :], in0=mean_dif[:, :], scalar=0.25, in1=mean_dif[:, :],
                                         op0=ALU.mult, op1=ALU.mult).then_inc(ln_terms, 1)
                dve.wait_ge(ln_terms, 3 * (n + 1))
                dve.tensor_tensor(veps[:, :], var_in[:, :], var_out[:, :], ALU.add).then_inc(ln_veps, 1)
                dve.wait_ge(ln_rstd, n + 1)
                for b in range(NB):
                    dve.tensor_scalar(nat[:, b, :], source(b), mean[:, b:b + 1], rstd[:, b:b + 1],
                                      ALU.subtract, ALU.mult).then_inc(nat_ready, 1)

            def layernorm_x(t):
                layernorm(t, lambda b: nat[:, b, :], lambda b: dve.wait_ge(x_loaded[b], 16 * (t + 1)))

            def x_los(t):
                for b in range(NB):
                    dve.wait_ge(x_hi, NB * t + b + 1)
                    dve.tensor_tensor(cur_lo[:, :, b * P:(b + 1) * P],
                                      bank[b][:, :].rearrange("p (k n) -> p k n", k=NK),
                                      f32(cur_hi[:, :, b * P:(b + 1) * P]), ALU.subtract).then_inc(x_split, 1)

            def elus(t):
                for m in range(NK):
                    dve.wait_ge(exp_done, NK * t + m + 1)
                    dve.tensor_scalar(tmp[:, m % 2, :], tmp[:, m % 2, :], 1.0, -1.0, ALU.min, ALU.add)\
                       .then_inc(expm1_done, 1)
                    dve.wait_ge(expm1_done, NK * t + m + 1)
                    dve.scalar_tensor_tensor(out=kcur[:, m, :], in0=bank[m][:, :], scalar=cols[:, BQK, m:m + 1],
                                             in1=tmp[:, m % 2, :], op0=ALU.add, op1=ALU.max).then_inc(kt_done, 1)

            def v_biases(t):
                for b in range(NB):
                    dve.wait_ge(v_ready, NB * t + b + 1)
                    dve.tensor_tensor(v_nat[:, b, :], bank[4 + b][:, :], bv_all, ALU.add).then_inc(v_biased, 1)

            def kv_add(t):
                dve.wait_ge(kv_ready, t + 1)
                dve.wait_ge(kv_added, t + 1)
                kv = bank[7][:, :].rearrange("p (m n) -> p m n", m=NK)
                for j in range(HALF):
                    own = slice(j * DH, (j + 1) * DH)
                    add = dve.tensor_tensor(kvblk[own, :, own], kvblk[own, :, own], kv[own, :, own], ALU.add)
                add.then_inc(kv_added, 1)

            dve.memset(kvblk[:, :, :], 0.0).then_inc(kv_added, 1)
            layernorm_x(0)
            split_matrix(0)
            x_los(0)
            dve.wait_ge(consts_loaded, 16 * 6)
            split_matrix(1)
            with dve.Fori(0, NT - 1) as t:
                elus(t)
                layernorm_x(t + 1)
                v_biases(t)
                x_los(t + 1)
                kv_add(t)
            elus(NT - 1)
            split_matrix(2)
            v_biases(NT - 1)
            split_matrix(3)
            kv_add(NT - 1)

            def y_product(s, m):
                dve.wait_ge(zg_done, NK * s + m + 1)
                slot = st[:, m, cols_of(s)]
                dve.tensor_tensor(slot, slot, tmp[:, m % 2, :], ALU.mult).then_inc(y_done, 1)

            def y_lo_part(s, m):
                dve.wait_ge(y_hi, NK * s + m + 1)
                dve.tensor_tensor(cur_lo[:, m, :], st[:, m, cols_of(s)], f32(cur_hi[:, m, :]), ALU.subtract)\
                   .then_inc(y_split, 1)

            def b_step(s, first_bank):
                layernorm(NT + s, lambda b: bank[first_bank + b][:, :], lambda b: dve.wait_ge(o_ready, NB * s + b + 1))
                for m in range(NK):
                    y_product(s, m)
                    if m >= 1:
                        y_lo_part(s, m - 1)
                y_lo_part(s, NK - 1)

            b_step(0, 4)
            with dve.Fori(1, NT - 1) as s:
                b_step(s, 0)
            for u in range(C_UNITS):
                split_chunk_unit(0, 0, u)
            b_step(NT - 1, 0)

            def h_product(n, t):
                dve.wait_ge(gate_done, n + 1)
                dve.wait_ge(up_ready, n + 1)
                dve.tensor_tensor(tmp[:, t % 2, :], tmp[:, t % 2, :], bank[2 * (t % 2) + 1][:, :], ALU.mult)\
                   .then_inc(h_done, 1)

            def h_lo_part(n, t):
                dve.wait_ge(h_hi, n + 1)
                dve.tensor_tensor(cur_lo[:, t % 2, :], tmp[:, t % 2, :], f32(cur_hi[:, t % 2, :]), ALU.subtract)\
                   .then_inc(h_split, 1)

            def c_chunk(c, r):
                last = isinstance(c, int) and c == NC - 1
                for t in range(NT):
                    n, nt = NT * c + t, (t + 1) % NT
                    if not (last and t == NT - 1):
                        h_product(n + 1, nt)
                    if not last and t < C_UNITS:
                        split_chunk_unit(c + 1, 1 - r, t)
                    if not (last and t == NT - 1):
                        h_lo_part(n + 1, nt)
                    for m in range(NK):
                        dve.wait_ge(f_ready, NK * n + m + 1)
                        dve.tensor_tensor(kf[:, m, cols_of(t)], kf[:, m, cols_of(t)], bank[4 + m][:, :], ALU.add)\
                           .then_inc(sums_taken, 1)
                    if last:
                        for m in range(NK):
                            dve.wait_ge(g_done, NK * t + m + 1)
                            dve.tensor_tensor(nat[:, m, :], nat[:, m, :], st[:, m, cols_of((t + 1) % NT)], ALU.mult)\
                               .then_inc(sg_done, 1)

            h_product(0, 0)
            h_lo_part(0, 0)
            dve.wait_ge(f_zeroed, 1)
            with dve.Fori(0, NC - 2, 2) as c:
                c_chunk(c, 0)
                c_chunk(c + 1, 1)
            c_chunk(NC - 2, 0)
            c_chunk(NC - 1, 1)

        @block.tensor
        def _(pe):
            def product(out, w, a, first, last):
                pe.matmul(out, w[0], a[0], start=first, stop=False)
                pe.matmul(out, w[0], a[1], start=False, stop=False)
                return pe.matmul(out, w[1], a[0], start=False, stop=last)

            def weight(r, k, m):
                return region_hi[r][:, k, m * P:(m + 1) * P], region_lo[r][:, k, m * P:(m + 1) * P]

            def xn(k, t):
                return xn_hi[:, k, cols_of(t)], xn_lo[:, k, cols_of(t)]

            def current(k, tokens=slice(0, TILE)):
                return cur_hi[:, k, tokens], cur_lo[:, k, tokens]

            def transpose_x(t):
                for b in range(NB):
                    pe.wait_ge(nat_ready, NB * t + b + 1)
                    for k in range(NK):
                        last = pe.transpose(bank[b][:, k * P:(k + 1) * P], nat[:, b, k * P:(k + 1) * P], ident[:, :])
                    last.then_inc(xt_ready, 1)

            def project_k(t):
                pe.wait_ge(x_split, NB * (t + 1))
                for m in range(NK):
                    for k in range(NK):
                        last = product(bank[m][:, :], weight(0, k, m), current(k), k == 0, k == NK - 1)
                    last.then_inc(kt_ready, 1)

            def project_v(t):
                pe.wait_ge(w_split, 2 * NK)
                for b in range(NB):
                    if b == NB - 1:
                        pe.wait_ge(kv_added, t + 1)
                    for k in range(NK):
                        last = product(bank[4 + b][:, :], current(k, slice(b * P, (b + 1) * P)),
                                       (region_hi[1][:, k, :], region_lo[1][:, k, :]), k == 0, k == NK - 1)
                    last.then_inc(v_ready, 1)

            def transpose_k(t):
                pe.wait_ge(kt_done, NK * (t + 1))
                for b in range(NB):
                    if b < NB - 1:
                        pe.wait_ge(v_biased, NB * t + b + 1)
                    elif not (isinstance(t, int) and t == NT - 1):
                        pe.wait_ge(x_split, NB * (t + 1) + 1)
                    out = bank[K_NAT_BANKS[b]]
                    for m in range(NK):
                        last = pe.transpose(out[:, m * P:(m + 1) * P], kcur[:, m, b * P:(b + 1) * P], ident[:, :])
                    last.then_inc(knat_ready, 1)

            def accumulate_kv(t):
                pe.wait_ge(v_done, NB * (t + 1))
                pe.wait_ge(knat_done, NB * (t + 1))
                for m in range(NK):
                    for b in range(NB):
                        last = pe.matmul(bank[7][:, m * P:(m + 1) * P], k_nat[:, b, m * P:(m + 1) * P],
                                         v_nat[:, b, m * P:(m + 1) * P], start=b == 0, stop=b == NB - 1)
                last.then_inc(kv_ready, 1)

            pe.wait_ge(ident_ready, 1)
            transpose_x(0)
            pe.wait_ge(w_split, NK)
            with pe.Fori(0, NT - 1) as t:
                project_k(t)
                project_v(t)
                pe.wait_ge(kt_done, NK * (t + 1))
                transpose_x(t + 1)
                transpose_k(t)
                accumulate_kv(t)
            project_k(NT - 1)
            project_v(NT - 1)
            transpose_k(NT - 1)
            accumulate_kv(NT - 1)

            def project_u(s, groups=range(NK)):
                tile = NT - 1 if isinstance(s, int) and s == 0 else s - 1
                for m in groups:
                    for k in range(NK):
                        last = product(bank[m][:, :], weight(0, k, m), xn(k, tile), k == 0, k == NK - 1)
                    last.then_inc(ut_ready, 1)

            def attend(b, out):
                for m in range(NK):
                    last = pe.matmul(out[:, m * P:(m + 1) * P], kcur[:, m, b * P:(b + 1) * P], kvblk[:, m, :],
                                     start=True, stop=True)
                last.then_inc(o_ready, 1)

            def transpose_z(s):
                pe.wait_ge(nat_ready, NB * (NT + s + 1))
                for m in range(NK):
                    if not (isinstance(s, int) and s == 0):
                        pe.wait_ge(s_done, NK * (s - 1) + m + 1)
                    for b in range(NB):
                        last = pe.transpose(bank[4 + m][:, b * P:(b + 1) * P], nat[:, b, m * P:(m + 1) * P], ident[:, :])
                    last.then_inc(zt_ready, 1)

            def project_s(s):
                for k in range(NK):
                    pe.wait_ge(y_split, NK * s + k + 1)
                    for m in range(NK):
                        if k == 0:
                            pe.wait_ge(zg_done, NK * s + m + 1)
                        last = product(bank[4 + m][:, :], weight(1, k, m), current(k), k == 0, k == NK - 1)
                        if k == NK - 1:
                            last.then_inc(s_ready, 1)

            def b_step(s):
                pe.wait_ge(ut_done, NK * s)
                project_u(s)
                pe.wait_ge(k_back, s)
                for b in range(NB):
                    pe.wait_ge(ut_done, NK * s + b + 1)
                    attend(b, bank[b])
                project_s(s - 1)
                transpose_z(s)

            pe.wait_ge(w_split, 3 * NK)
            pe.wait_ge(xn_kept, 2 * NT)
            project_u(0, range(0, 2))
            pe.wait_ge(kv_added, NT + 1)
            for b in range(NB):
                attend(b, bank[4 + b])
            project_u(0, range(2, NK))
            transpose_z(0)
            pe.wait_ge(w_split, 4 * NK)
            with pe.Fori(1, NT) as s:
                b_step(s)

            def ffn_in(c, r, t):
                for u, sem_of in ((0, gate_ready), (1, up_ready)):
                    if t == 0:
                        pe.wait_ge(w_split, chunk_units(c) + u + 1)
                    for k in range(NK):
                        last = product(bank[2 * (t % 2) + u][:, :],
                                       (region_hi[r][:, u, k * P:(k + 1) * P], region_lo[r][:, u, k * P:(k + 1) * P]),
                                       xn(k, t), k == 0, k == NK - 1)
                    last.then_inc(sem_of, 1)

            def ffn_out(c, r, t):
                n = NT * c + t
                if t == 0:
                    pe.wait_ge(w_split, chunk_units(c) + C_UNITS)
                pe.wait_ge(h_split, n + 1)
                for m in range(NK):
                    pe.wait_ge(sums_taken, NK * n + m + 1)
                    product(bank[4 + m][:, :],
                            (region_hi[r][:, 2, m * P:(m + 1) * P], region_lo[r][:, 2, m * P:(m + 1) * P]),
                            current(t % 2), True, True).then_inc(f_ready, 1)

            def c_chunk(c, r):
                last = isinstance(c, int) and c == NC - 1
                for t in range(NT):
                    if t < NT - 1:
                        ffn_in(c, r, t + 1)
                    elif not last:
                        ffn_in(c + 1, 1 - r, 0)
                    ffn_out(c, r, t)

            ffn_in(0, 0, 0)
            project_s(NT - 1)
            with pe.Fori(0, NC - 2, 2) as c:
                c_chunk(c, 0)
                c_chunk(c + 1, 1)
            c_chunk(NC - 2, 0)
            c_chunk(NC - 1, 1)


K_NAT_BANKS = (4, 5, 6, 0)


def kernel(L0_attn_x, L0_attn_Wqk, L0_attn_bqk, L0_attn_Wv, L0_attn_bv, L0_attn_Wu, L0_attn_bu, L0_attn_Wo,
           L0_attn_bo, L0_attn_ln_g, L0_attn_ln_b, L0_ffn_w_gate, L0_ffn_w_up, L0_ffn_w_down):
    import concourse.bacc as bacc
    from concourse.bass_utils import run_bass_kernel_spmd

    x = np.asarray(L0_attn_x)
    _, n, d = x.shape
    nk, nc_ = d // P, L0_ffn_w_gate.shape[0] // P

    def by_group(v):
        return np.ascontiguousarray(np.asarray(v).reshape(nk, P).T)

    def rows(w):
        return np.ascontiguousarray(np.asarray(w).reshape(nk, P, -1))

    def chunks_in(w):
        w = np.asarray(w).reshape(nc_, P, nk, P)
        return np.ascontiguousarray(w.transpose(0, 3, 2, 1)).reshape(nc_, P, nk * P)

    arrays = {
        "x": np.ascontiguousarray(x[0]),
        "xT": np.ascontiguousarray(x[0].T.reshape(nk, P, n).transpose(1, 0, 2)),
        "wqk": rows(L0_attn_Wqk), "wv": rows(L0_attn_Wv), "wu": rows(L0_attn_Wu), "wo": rows(L0_attn_Wo),
        "wg": chunks_in(L0_ffn_w_gate), "wup": chunks_in(L0_ffn_w_up),
        "wd": np.ascontiguousarray(np.asarray(L0_ffn_w_down).T).reshape(nc_, P, d),
        "bqk": by_group(L0_attn_bqk), "bu": by_group(L0_attn_bu), "bo": by_group(L0_attn_bo),
        "ln_g": by_group(L0_attn_ln_g), "ln_b": by_group(L0_attn_ln_b),
        "bv": np.ascontiguousarray(np.asarray(L0_attn_bv)),
    }
    nc = bacc.Bacc("TRN2", target_bir_lowering=False, num_devices=1)
    args = {name: nc.dram_tensor(f"in_{name}", a.shape, mybir.dt.from_np(a.dtype), kind="ExternalInput").ap()
            for name, a in arrays.items()}
    outT = nc.dram_tensor("outT", (P, nk, n), F32, kind="ExternalOutput").ap()
    build(nc, **args, outT=outT)
    r = run_bass_kernel_spmd(nc, [{f"in_{name}": a for name, a in arrays.items()}], core_ids=[0])
    got = r.results[0]["outT"]
    return np.ascontiguousarray(got.transpose(2, 1, 0)).reshape(1, n, d)
```

```python
from contextlib import ExitStack

import numpy as np

import concourse.bass as bass
from concourse import mybir
from concourse.alu_op_type import AluOpType as ALU

ACT = mybir.ActivationFunctionType
F32 = mybir.dt.float32
F32R = mybir.dt.float32r

P = 128
TILE = 512
EPS = 1e-5
WARM_UP, WARM_UP_X = 20, 9
DH = 32


def build(nc, x, xT, wqk, wv, wu, wo, wg, wup, wd, bqk, bu, bo, ln_g, ln_b, bv, outT):
    N, D = x.shape
    NT = N // TILE
    NB = TILE // P
    NK = D // P
    NC = wg.shape[0]
    assert D == TILE and NT == 4 and NB == 4 and NK == 4 and NC % 2 == 0
    W_UNITS = 4 * NK
    C_UNITS = 3
    HALF = P // DH

    ctx = ExitStack()
    with ctx:
        def sb(name, shape, dt=F32):
            return ctx.enter_context(nc.sbuf_tensor(name, shape, dt))

        def sem(name):
            return ctx.enter_context(nc.semaphore(name))

        xn_hi = sb("xn_hi", [P, NK, N], F32R)
        xn_lo = sb("xn_lo", [P, NK, N], F32R)
        kf = sb("kf", [P, NK, N])
        st = sb("st", [P, NK, N])
        region_hi = [sb(f"region{r}_hi", [P, NK, TILE], F32R) for r in range(2)]
        region_lo = [sb(f"region{r}_lo", [P, NK, TILE], F32R) for r in range(2)]
        stage = sb("stage", [P, NK, TILE])
        cur_hi = sb("cur_hi", [P, NK, TILE], F32R)
        cur_lo = sb("cur_lo", [P, NK, TILE], F32R)
        kcur = sb("kcur", [P, NK, TILE])
        nat = sb("nat", [P, NB, TILE])
        tmp = sb("tmp", [P, 2, TILE])
        kvblk = sb("kvblk", [P, NK, P])
        cols = sb("cols", [P, 5, NK])
        ident = sb("ident", [P, P])
        stats = sb("stats", [P, NB, 6])
        mean, mean_sum, mean_dif, dev_sum, var_in, var_out = (
            sb(name, [P, NB]) for name in ("mean", "mean_sum", "mean_dif", "dev_sum", "var_in", "var_out"))
        veps = sb("veps", [P, NB])
        rstd = sb("rstd", [P, NB])
        half = sb("half", [P, NB])
        k_nat = st[:, :, 3 * TILE:4 * TILE]
        v_nat = st[:, :, TILE:2 * TILE]
        bv_all = st[:, 0, 2 * TILE:3 * TILE]
        xt_buffer = (kcur, stage, nat)
        BQK, BU, BO, LNG, LNB = range(5)
        bank = [ctx.enter_context(nc.psum_tensor(f"bank{b}", [P, TILE], F32)) for b in range(8)]

        consts_loaded = sem("consts_loaded")
        x_loaded = [sem(f"x_loaded{b}") for b in range(NB)]
        w_loaded = [sem(f"w_loaded{k}") for k in range(NK)]
        xt_loaded = [sem(f"xt_loaded{i}") for i in range(3)]
        out_stored = sem("out_stored")
        ident_zeroed = sem("ident_zeroed")
        ident_ready = sem("ident_ready")
        half_ready = sem("half_ready")
        w_hi = sem("w_hi")
        w_split = sem("w_split")
        ln_stats = sem("ln_stats")
        ln_halves = sem("ln_halves")
        ln_terms = sem("ln_terms")
        ln_veps = sem("ln_veps")
        ln_rstd = sem("ln_rstd")
        nat_ready = sem("nat_ready")
        xt_ready = sem("xt_ready")
        x_hi = sem("x_hi")
        x_split = sem("x_split")
        xn_kept = sem("xn_kept")
        kt_ready = sem("kt_ready")
        k_clamped = sem("k_clamped")
        exp_done = sem("exp_done")
        expm1_done = sem("expm1_done")
        kt_done = sem("kt_done")
        v_ready = sem("v_ready")
        v_biased = sem("v_biased")
        v_done = sem("v_done")
        knat_ready = sem("knat_ready")
        knat_done = sem("knat_done")
        kv_ready = sem("kv_ready")
        kv_added = sem("kv_added")
        k_kept = sem("k_kept")
        k_back = sem("k_back")
        f_zeroed = sem("f_zeroed")
        ut_ready = sem("ut_ready")
        ut_done = sem("ut_done")
        o_ready = sem("o_ready")
        zt_ready = sem("zt_ready")
        zg_done = sem("zg_done")
        y_done = sem("y_done")
        y_hi = sem("y_hi")
        y_split = sem("y_split")
        s_ready = sem("s_ready")
        s_done = sem("s_done")
        gate_ready = sem("gate_ready")
        up_ready = sem("up_ready")
        gate_done = sem("gate_done")
        h_done = sem("h_done")
        h_hi = sem("h_hi")
        h_split = sem("h_split")
        f_ready = sem("f_ready")
        sums_taken = sem("sums_taken")
        g_done = sem("g_done")
        sg_done = [sem(f"sg_done{i}") for i in range(2)]
        out_done = [sem(f"out_done{i}") for i in range(2)]

        block = ctx.enter_context(nc.Block())

        def f32(ap):
            return ap.bitcast(F32)

        def wait_alone(eng, semaphore, value):
            eng.wait_ge(ident_ready, 1)
            eng.wait_ge(semaphore, value)

        def cols_of(t):
            return bass.ds(t * TILE, TILE)

        def chunk_units(c):
            return W_UNITS + C_UNITS * c

        def finish_out(eng, t, groups, times, plus):
            for m in groups:
                eng.wait_ge(g_done, NK * t + m + 1)
                eng.tensor_tensor(kf[:, m, cols_of(t)], kf[:, m, cols_of(t)], st[:, m, cols_of((t + 1) % NT)], ALU.mult)\
                   .then_inc(times, 1)
            eng.wait_ge(xt_loaded[t % 3], 16 * (t // 3 + 1))
            for i, m in enumerate(groups):
                eng.wait_ge(times, len(groups) * t + i + 1)
                eng.tensor_tensor(kf[:, m, cols_of(t)], kf[:, m, cols_of(t)], xt_buffer[t % 3][:, m, :], ALU.add)\
                   .then_inc(plus, 1)

        @block.sync
        def _(sp):
            def load_x(t, block_of_tile):
                sp.dma_start(nat[:, block_of_tile, :], x[bass.ds(t * TILE + block_of_tile * P, P), :])\
                  .then_inc(x_loaded[block_of_tile], 16)

            def load_w(dram, k):
                sp.dma_start(stage[:, k, :], dram[k, :, :]).then_inc(w_loaded[k], 16)

            def load_chunk(c):
                for u, dram in enumerate((wg, wup, wd)):
                    sp.wait_ge(w_split, chunk_units(c) - C_UNITS + u + 1)
                    sp.dma_start(stage[:, u, :], dram[bass.ds(c, 1), :, :].rearrange("a p n -> p (a n)"))\
                      .then_inc(w_loaded[u], 16)

            for b in range(NB):
                load_x(0, b)
            for k in range(NK):
                load_w(wqk, k)
            for dst, src in ((cols[:, BQK, :], bqk), (cols[:, BU, :], bu), (cols[:, BO, :], bo),
                             (cols[:, LNG, :], ln_g), (cols[:, LNB, :], ln_b), (bv_all, bv.partition_broadcast(P))):
                sp.dma_start(dst, src).then_inc(consts_loaded, 16)
            for k in range(NK):
                sp.wait_ge(w_split, k + 1)
                load_w(wv, k)

            def keep_tile(t):
                sp.wait_ge(x_split, NB * (t + 1))
                sp.dma_start(f32(xn_hi[:, :, cols_of(t)]), f32(cur_hi[:, :, :])).then_inc(xn_kept, 16)
                sp.dma_start(f32(xn_lo[:, :, cols_of(t)]), f32(cur_lo[:, :, :])).then_inc(xn_kept, 16)

            with sp.Fori(0, NT - 1) as t:
                keep_tile(t)
                sp.wait_ge(xt_ready, NB * (t + 1))
                for b in range(NB):
                    load_x(t + 1, b)
            for k in range(NK):
                sp.wait_ge(w_split, NK + k + 1)
                load_w(wu, k)
            keep_tile(NT - 1)
            for k in range(NK):
                sp.wait_ge(w_split, 2 * NK + k + 1)
                load_w(wo, k)
            for u, dram in enumerate((wg, wup, wd)):
                sp.wait_ge(w_split, W_UNITS - NK + u + 1)
                sp.dma_start(stage[:, u, :], dram[0, :, :]).then_inc(w_loaded[u], 16)
            with sp.Fori(0, NT - 1) as s:
                sp.wait_ge(o_ready, NB * (s + 1))
                sp.dma_start(kcur[:, :, :], kf[:, :, cols_of(s)]).then_inc(k_back, 16)
            with sp.Fori(1, NC) as c:
                load_chunk(c)
            def load_xt(t):
                sp.dma_start(xt_buffer[t % 3][:, :, :], xT[:, :, t * TILE:(t + 1) * TILE]).then_inc(xt_loaded[t % 3], 16)

            sp.wait_ge(o_ready, NB * NT)
            load_xt(0)
            sp.wait_ge(w_split, chunk_units(NC))
            load_xt(1)
            sp.wait_ge(zt_ready, NK * NT)
            load_xt(2)
            for t in range(NT):
                for m in (2, 0, 3, 1):
                    sp.wait_ge(out_done[m // 2], NK // 2 * t + m % 2 + 1)
                    sp.dma_start(outT[:, m, t * TILE:(t + 1) * TILE], kf[:, m, t * TILE:(t + 1) * TILE])\
                      .then_inc(out_stored, 16)
                if t + 3 < NT:
                    load_xt(t + 3)
            sp.wait_ge(out_stored, 16 * NK * NT)

        @block.gpsimd
        def _(pool):
            def power(n):
                pool.wait_ge(ln_veps, n + 1)
                pool.tensor_tensor(rstd[:, :], veps[:, :], half[:, :], ALU.pow).then_inc(ln_rstd, 1)

            pool.memset(half[:, :], -0.5).then_inc(half_ready, 1)
            pool.memset(ident[:, :], 0.0).then_inc(ident_zeroed, 1)
            pool.wait_ge(ident_zeroed, 1)
            pool.affine_select(out=ident[:, :], in_=ident[:, :], compare_op=ALU.not_equal, fill=1.0,
                               base=0, pattern=[[-1, P]], channel_multiplier=1).then_inc(ident_ready, 1)
            pool.wait_ge(half_ready, 1)
            power(0)
            with pool.Fori(1, 2 * NT - 1) as n:
                power(n)
            pool.wait_ge(k_back, 16 * (NT - 1))
            pool.memset(kf[:, :, :], 0.0).then_inc(f_zeroed, 1)
            power(2 * NT - 1)
            for t in range(NT):
                finish_out(pool, t, range(0, NK // 2), sg_done[0], out_done[0])

        @block.scalar
        def _(act):
            def split_hi(slot, dst, loaded):
                act.wait_ge(w_loaded[slot], loaded)
                act.activation(dst, stage[:, slot, :], ACT.Copy).then_inc(w_hi, 1)

            def split_matrix(j):
                for k in range(NK):
                    split_hi(k, region_hi[j % 2][:, k, :], 16 * (j + 1))

            def split_chunk_unit(c, r, u):
                split_hi(u, region_hi[r][:, u, :], 16 * (c + 5))

            def x_his(t):
                for b in range(NB):
                    act.wait_ge(xt_ready, NB * t + b + 1)
                    if not (isinstance(t, int) and t == 0) and b == 0:
                        act.wait_ge(xn_kept, 32 * t)
                    act.activation(cur_hi[:, :, b * P:(b + 1) * P],
                                   bank[b][:, :].rearrange("p (k n) -> p k n", k=NK), ACT.Copy).then_inc(x_hi, 1)

            def exps(t):
                for m in range(NK):
                    act.wait_ge(k_clamped, NK * t + m + 1)
                    act.activation(tmp[:, m % 2, :], tmp[:, m % 2, :], ACT.Exp).then_inc(exp_done, 1)

            def v_silus(t):
                for b in range(NB):
                    act.wait_ge(v_biased, NB * t + b + 1)
                    act.activation(v_nat[:, b, :], v_nat[:, b, :], ACT.Silu).then_inc(v_done, 1)

            def k_nats(t):
                for b in range(NB):
                    act.wait_ge(knat_ready, NB * t + b + 1)
                    act.activation(k_nat[:, b, :], bank[b][:, :], ACT.Copy).then_inc(knat_done, 1)

            split_matrix(0)
            x_his(0)
            act.wait_ge(consts_loaded, 16 * 6)
            split_matrix(1)
            with act.Fori(0, NT - 1) as t:
                exps(t)
                k_nats(t)
                act.dma_start(kf[:, :, cols_of(t)], kcur[:, :, :]).then_inc(k_kept, 16)
                v_silus(t)
                x_his(t + 1)
            exps(NT - 1)
            split_matrix(2)
            k_nats(NT - 1)
            v_silus(NT - 1)
            split_matrix(3)

            def u_silus(s):
                for m in range(NK):
                    wait_alone(act, ut_ready, NK * s + m + 1)
                    act.activation(st[:, m, cols_of(s)], bank[m][:, :], ACT.Silu, bias=cols[:, BU, m:m + 1])\
                       .then_inc(ut_done, 1)

            def s_biases(s, done):
                for m in range(NK):
                    wait_alone(act, s_ready, NK * s + m + 1)
                    act.activation(st[:, m, cols_of(s)], bank[4 + m][:, :], ACT.Identity,
                                   bias=cols[:, BO, m:m + 1]).then_inc(done, 1)

            def y_hi_part(s, m):
                wait_alone(act, y_done, NK * s + m + 1)
                act.activation(cur_hi[:, m, :], st[:, m, cols_of(s)], ACT.Copy).then_inc(y_hi, 1)

            def zg_and_y_hi(s):
                for m in range(NK):
                    act.wait_ge(zt_ready, NK * s + m + 1)
                    act.activation(tmp[:, m % 2, :], bank[4 + m][:, :], ACT.Identity,
                                   bias=cols[:, LNB, m:m + 1], scale=cols[:, LNG, m:m + 1]).then_inc(zg_done, 1)
                    if m >= 1:
                        y_hi_part(s, m - 1)
                y_hi_part(s, NK - 1)

            u_silus(0)
            act.wait_ge(xn_kept, 32 * NT)
            zg_and_y_hi(0)
            with act.Fori(1, NT - 1) as s:
                u_silus(s)
                s_biases(s - 1, s_done)
                zg_and_y_hi(s)
            u_silus(NT - 1)
            for u in range(C_UNITS):
                split_chunk_unit(0, 0, u)
            s_biases(NT - 2, s_done)
            zg_and_y_hi(NT - 1)

            def gate_silu(n, t):
                act.wait_ge(gate_ready, n + 1)
                act.activation(tmp[:, t % 2, :], bank[2 * (t % 2)][:, :], ACT.Silu).then_inc(gate_done, 1)

            def h_hi_part(n, t):
                act.wait_ge(h_done, n + 1)
                act.activation(cur_hi[:, t % 2, :], tmp[:, t % 2, :], ACT.Copy).then_inc(h_hi, 1)

            def c_chunk(c, r):
                last = isinstance(c, int) and c == NC - 1
                for t in range(NT):
                    n, nt = NT * c + t, (t + 1) % NT
                    if not (last and t == NT - 1):
                        gate_silu(n + 1, nt)
                        h_hi_part(n + 1, nt)
                    if not last and t < C_UNITS:
                        split_chunk_unit(c + 1, 1 - r, t)
                    if last:
                        for m in range(NK):
                            act.wait_ge(sums_taken, NK * (n + 1) + m + 1)
                            act.activation(kf[:, m, cols_of(t)], kf[:, m, cols_of(t)], ACT.Silu).then_inc(g_done, 1)

            gate_silu(0, 0)
            act.wait_ge(s_ready, NK * NT)
            h_hi_part(0, 0)
            s_biases(NT - 1, sums_taken)
            with act.Fori(0, NC - 2, 2) as c:
                c_chunk(c, 0)
                c_chunk(c + 1, 1)
            c_chunk(NC - 2, 0)
            c_chunk(NC - 1, 1)

        @block.vector
        def _(dve):
            def split_lo(unit, slot, hi, lo):
                dve.wait_ge(w_hi, unit + 1)
                dve.tensor_tensor(lo, stage[:, slot, :], f32(hi), ALU.subtract).then_inc(w_split, 1)

            def split_matrix(j, units=range(NK)):
                for k in units:
                    split_lo(NK * j + k, k, region_hi[j % 2][:, k, :], region_lo[j % 2][:, k, :])

            def split_chunk_unit(c, r, u):
                split_lo(chunk_units(c) + u, u, region_hi[r][:, u, :], region_lo[r][:, u, :])

            def layernorm(n, source, arrived, meanwhile=None):
                for b in range(NB):
                    arrived(b)
                    dve.bn_stats(stats[:, b, :], source(b)).then_inc(ln_stats, 1)
                mean_e, dev_e, mean_o, dev_o = (stats[:, :, i] for i in (1, 2, 4, 5))
                dve.wait_ge(ln_stats, NB * (n + 1))
                dve.tensor_tensor(mean_sum[:, :], mean_e, mean_o, ALU.add).then_inc(ln_halves, 1)
                dve.tensor_tensor(mean_dif[:, :], mean_e, mean_o, ALU.subtract).then_inc(ln_halves, 1)
                dve.tensor_tensor(dev_sum[:, :], dev_e, dev_o, ALU.add).then_inc(ln_halves, 1)
                dve.wait_ge(ln_halves, 3 * (n + 1))
                dve.tensor_scalar(mean[:, :], mean_sum[:, :], 0.5, None, ALU.mult).then_inc(ln_terms, 1)
                dve.tensor_scalar(var_in[:, :], dev_sum[:, :], 1.0 / D, EPS, ALU.mult, ALU.add).then_inc(ln_terms, 1)
                dve.scalar_tensor_tensor(out=var_out[:, :], in0=mean_dif[:, :], scalar=0.25, in1=mean_dif[:, :],
                                         op0=ALU.mult, op1=ALU.mult).then_inc(ln_terms, 1)
                dve.wait_ge(ln_terms, 3 * (n + 1))
                dve.tensor_tensor(veps[:, :], var_in[:, :], var_out[:, :], ALU.add).then_inc(ln_veps, 1)
                if meanwhile:
                    meanwhile()
                dve.wait_ge(ln_rstd, n + 1)
                for b in range(NB):
                    dve.tensor_scalar(nat[:, b, :], source(b), mean[:, b:b + 1], rstd[:, b:b + 1],
                                      ALU.subtract, ALU.mult).then_inc(nat_ready, 1)

            def layernorm_x(t, meanwhile=None):
                layernorm(t, lambda b: nat[:, b, :], lambda b: dve.wait_ge(x_loaded[b], 16 * (t + 1)), meanwhile)

            def x_los(t):
                for b in range(NB):
                    dve.wait_ge(x_hi, NB * t + b + 1)
                    dve.tensor_tensor(cur_lo[:, :, b * P:(b + 1) * P],
                                      bank[b][:, :].rearrange("p (k n) -> p k n", k=NK),
                                      f32(cur_hi[:, :, b * P:(b + 1) * P]), ALU.subtract).then_inc(x_split, 1)

            def elus(t):
                def clamp(m):
                    if m >= 2:
                        dve.wait_ge(kt_done, NK * t + m - 1)
                    dve.wait_ge(kt_ready, NK * t + m + 1)
                    dve.tensor_scalar(tmp[:, m % 2, :], bank[m][:, :], cols[:, BQK, m:m + 1], 0.0, ALU.add, ALU.min)\
                       .then_inc(k_clamped, 1)

                clamp(0)
                for m in range(NK):
                    if m + 1 < NK:
                        clamp(m + 1)
                    dve.wait_ge(exp_done, NK * t + m + 1)
                    dve.tensor_scalar(tmp[:, m % 2, :], tmp[:, m % 2, :], -1.0, None, ALU.add).then_inc(expm1_done, 1)
                    dve.wait_ge(expm1_done, NK * t + m + 1)
                    dve.scalar_tensor_tensor(out=kcur[:, m, :], in0=bank[m][:, :], scalar=cols[:, BQK, m:m + 1],
                                             in1=tmp[:, m % 2, :], op0=ALU.add, op1=ALU.max).then_inc(kt_done, 1)

            def v_biases(t):
                for b in range(NB):
                    dve.wait_ge(v_ready, NB * t + b + 1)
                    dve.tensor_tensor(v_nat[:, b, :], bank[4 + b][:, :], bv_all, ALU.add).then_inc(v_biased, 1)

            def kv_add(t):
                dve.wait_ge(kv_ready, t + 1)
                dve.wait_ge(kv_added, t + 1)
                kv = bank[7][:, :].rearrange("p (m n) -> p m n", m=NK)
                for j in range(HALF):
                    own = slice(j * DH, (j + 1) * DH)
                    add = dve.tensor_tensor(kvblk[own, :, own], kvblk[own, :, own], kv[own, :, own], ALU.add)
                add.then_inc(kv_added, 1)

            dve.memset(kvblk[:, :, :], 0.0).then_inc(kv_added, 1)
            layernorm_x(0, lambda: split_matrix(0, range(0, 2)))
            x_los(0)
            split_matrix(0, range(2, NK))
            dve.wait_ge(consts_loaded, 16 * 6)
            split_matrix(1)
            with dve.Fori(0, NT - 1) as t:
                elus(t)
                layernorm_x(t + 1)
                v_biases(t)
                x_los(t + 1)
                kv_add(t)
                dve.wait_ge(k_kept, 16 * (t + 1))
            elus(NT - 1)
            split_matrix(2)
            v_biases(NT - 1)
            split_matrix(3)
            kv_add(NT - 1)

            def y_product(s, m):
                dve.wait_ge(zg_done, NK * s + m + 1)
                slot = st[:, m, cols_of(s)]
                dve.tensor_tensor(slot, slot, tmp[:, m % 2, :], ALU.mult).then_inc(y_done, 1)

            def y_lo_part(s, m):
                dve.wait_ge(y_hi, NK * s + m + 1)
                dve.tensor_tensor(cur_lo[:, m, :], st[:, m, cols_of(s)], f32(cur_hi[:, m, :]), ALU.subtract)\
                   .then_inc(y_split, 1)

            def b_step(s, first_bank):
                layernorm(NT + s, lambda b: bank[first_bank + b][:, :], lambda b: dve.wait_ge(o_ready, NB * s + b + 1))
                for m in range(NK):
                    y_product(s, m)
                    if m >= 1:
                        y_lo_part(s, m - 1)
                y_lo_part(s, NK - 1)

            b_step(0, 4)
            with dve.Fori(1, NT - 1) as s:
                b_step(s, 0)
            for u in range(C_UNITS):
                split_chunk_unit(0, 0, u)
            b_step(NT - 1, 0)

            def h_product(n, t):
                dve.wait_ge(gate_done, n + 1)
                dve.wait_ge(up_ready, n + 1)
                dve.tensor_tensor(tmp[:, t % 2, :], tmp[:, t % 2, :], bank[2 * (t % 2) + 1][:, :], ALU.mult)\
                   .then_inc(h_done, 1)

            def h_lo_part(n, t):
                dve.wait_ge(h_hi, n + 1)
                dve.tensor_tensor(cur_lo[:, t % 2, :], tmp[:, t % 2, :], f32(cur_hi[:, t % 2, :]), ALU.subtract)\
                   .then_inc(h_split, 1)

            def f_add(n, t):
                for m in range(NK):
                    dve.wait_ge(f_ready, NK * n + m + 1)
                    dve.tensor_tensor(kf[:, m, cols_of(t)], kf[:, m, cols_of(t)], bank[4 + m][:, :], ALU.add)\
                       .then_inc(sums_taken, 1)

            def c_chunk(c, r):
                last = isinstance(c, int) and c == NC - 1
                for t in range(NT):
                    n, nt = NT * c + t, (t + 1) % NT
                    if not (last and t == NT - 1):
                        h_product(n + 1, nt)
                    if not last and t < C_UNITS:
                        split_chunk_unit(c + 1, 1 - r, t)
                    if not (last and t == NT - 1):
                        h_lo_part(n + 1, nt)
                    if not (last and t == NT - 1):
                        f_add(n, t)
                    if last and t == NT - 2:
                        f_add(n + 1, t + 1)
                    if last:
                        finish_out(dve, t, range(NK // 2, NK), sg_done[1], out_done[1])

            h_product(0, 0)
            h_lo_part(0, 0)
            dve.wait_ge(f_zeroed, 1)
            with dve.Fori(0, NC - 2, 2) as c:
                c_chunk(c, 0)
                c_chunk(c + 1, 1)
            c_chunk(NC - 2, 0)
            c_chunk(NC - 1, 1)

        @block.tensor
        def _(pe):
            def product(out, w, a, first, last):
                pe.matmul(out, w[0], a[0], start=first, stop=False)
                pe.matmul(out, w[0], a[1], start=False, stop=False)
                return pe.matmul(out, w[1], a[0], start=False, stop=last)

            def weight(r, k, m):
                return region_hi[r][:, k, m * P:(m + 1) * P], region_lo[r][:, k, m * P:(m + 1) * P]

            def xn(k, t):
                return xn_hi[:, k, cols_of(t)], xn_lo[:, k, cols_of(t)]

            def current(k, tokens=slice(0, TILE)):
                return cur_hi[:, k, tokens], cur_lo[:, k, tokens]

            def keep_warm(products):
                for _ in range(products):
                    pe.matmul(bank[7][:, 0:P], ident[:, :], ident[:, :], start=True, stop=True)

            def transpose_x(t):
                for b in range(NB):
                    if not (isinstance(t, int) and t == 0):
                        pe.wait_ge(knat_done, NB * (t - 1) + b + 1)
                    pe.wait_ge(nat_ready, NB * t + b + 1)
                    for k in range(NK):
                        last = pe.transpose(bank[b][:, k * P:(k + 1) * P], nat[:, b, k * P:(k + 1) * P], ident[:, :])
                    last.then_inc(xt_ready, 1)

            def project_k(t):
                pe.wait_ge(x_split, NB * (t + 1))
                for m in range(NK):
                    for k in range(NK):
                        if m == 0:
                            pe.wait_ge(w_split, k + 1)
                        last = product(bank[m][:, :], weight(0, k, m), current(k), k == 0, k == NK - 1)
                    last.then_inc(kt_ready, 1)

            def project_v(t, blocks):
                pe.wait_ge(w_split, 2 * NK)
                for b in blocks:
                    if b == NB - 1:
                        pe.wait_ge(kv_added, t + 1)
                    for k in range(NK):
                        last = product(bank[4 + b][:, :], current(k, slice(b * P, (b + 1) * P)),
                                       (region_hi[1][:, k, :], region_lo[1][:, k, :]), k == 0, k == NK - 1)
                    last.then_inc(v_ready, 1)

            def transpose_k(t):
                pe.wait_ge(kt_done, NK * (t + 1))
                for b in range(NB):
                    for m in range(NK):
                        last = pe.transpose(bank[b][:, m * P:(m + 1) * P], kcur[:, m, b * P:(b + 1) * P], ident[:, :])
                    last.then_inc(knat_ready, 1)

            def accumulate_kv(t):
                pe.wait_ge(v_done, NB * (t + 1))
                pe.wait_ge(knat_done, NB * (t + 1))
                for m in range(NK):
                    for b in range(NB):
                        last = pe.matmul(bank[7][:, m * P:(m + 1) * P], k_nat[:, b, m * P:(m + 1) * P],
                                         v_nat[:, b, m * P:(m + 1) * P], start=b == 0, stop=b == NB - 1)
                last.then_inc(kv_ready, 1)

            pe.wait_ge(ident_ready, 1)
            keep_warm(WARM_UP)
            transpose_x(0)
            keep_warm(WARM_UP_X)
            def k_and_v(t):
                project_k(t)
                project_v(t, range(0, 2))
                transpose_k(t)
                project_v(t, range(2, NB))

            with pe.Fori(0, NT - 1) as t:
                k_and_v(t)
                transpose_x(t + 1)
                accumulate_kv(t)
            k_and_v(NT - 1)

            def project_u(groups, xn_of):
                for m in groups:
                    for k in range(NK):
                        last = product(bank[m][:, :], weight(0, k, m), xn_of(k), k == 0, k == NK - 1)
                    last.then_inc(ut_ready, 1)

            def attend(b, out):
                for m in range(NK):
                    last = pe.matmul(out[:, m * P:(m + 1) * P], kcur[:, m, b * P:(b + 1) * P], kvblk[:, m, :],
                                     start=True, stop=True)
                last.then_inc(o_ready, 1)

            def transpose_z(s):
                pe.wait_ge(nat_ready, NB * (NT + s + 1))
                for m in range(NK):
                    if not (isinstance(s, int) and s == 0):
                        pe.wait_ge(s_done, NK * (s - 1) + m + 1)
                    for b in range(NB):
                        last = pe.transpose(bank[4 + m][:, b * P:(b + 1) * P], nat[:, b, m * P:(m + 1) * P], ident[:, :])
                    last.then_inc(zt_ready, 1)

            def project_s(s):
                for k in range(NK):
                    pe.wait_ge(y_split, NK * s + k + 1)
                    for m in range(NK):
                        if k == 0:
                            pe.wait_ge(zg_done, NK * s + m + 1)
                        last = product(bank[4 + m][:, :], weight(1, k, m), current(k), k == 0, k == NK - 1)
                        if k == NK - 1:
                            last.then_inc(s_ready, 1)

            def b_step(s):
                pe.wait_ge(ut_done, NK * s)
                project_u(range(NK), lambda k: xn(k, s - 1))
                pe.wait_ge(k_back, 16 * s)
                for b in range(NB):
                    pe.wait_ge(ut_done, NK * s + b + 1)
                    attend(b, bank[b])
                project_s(s - 1)
                transpose_z(s)

            pe.wait_ge(w_split, 3 * NK)
            pe.wait_ge(knat_done, NB * NT)
            project_u(range(0, 1), current)
            accumulate_kv(NT - 1)
            project_u(range(1, 2), current)
            pe.wait_ge(kv_added, NT + 1)
            for b in range(NB):
                attend(b, bank[4 + b])
            project_u(range(2, NK), current)
            transpose_z(0)
            pe.wait_ge(xn_kept, 32 * NT)
            pe.wait_ge(w_split, 4 * NK)
            with pe.Fori(1, NT) as s:
                b_step(s)

            def ffn_in(c, r, t):
                for u, sem_of in ((0, gate_ready), (1, up_ready)):
                    if t == 0:
                        pe.wait_ge(w_split, chunk_units(c) + u + 1)
                    for k in range(NK):
                        last = product(bank[2 * (t % 2) + u][:, :],
                                       (region_hi[r][:, u, k * P:(k + 1) * P], region_lo[r][:, u, k * P:(k + 1) * P]),
                                       xn(k, t), k == 0, k == NK - 1)
                    last.then_inc(sem_of, 1)

            def ffn_out(c, r, t):
                n = NT * c + t
                if t == 0:
                    pe.wait_ge(w_split, chunk_units(c) + C_UNITS)
                pe.wait_ge(h_split, n + 1)
                for m in range(NK):
                    pe.wait_ge(sums_taken, NK * n + m + 1)
                    product(bank[4 + m][:, :],
                            (region_hi[r][:, 2, m * P:(m + 1) * P], region_lo[r][:, 2, m * P:(m + 1) * P]),
                            current(t % 2), True, True).then_inc(f_ready, 1)

            def c_chunk(c, r):
                last = isinstance(c, int) and c == NC - 1
                for t in range(NT):
                    if t < NT - 1:
                        ffn_in(c, r, t + 1)
                    elif not last:
                        ffn_in(c + 1, 1 - r, 0)
                    ffn_out(c, r, t)

            ffn_in(0, 0, 0)
            project_s(NT - 1)
            with pe.Fori(0, NC - 2, 2) as c:
                c_chunk(c, 0)
                c_chunk(c + 1, 1)
            c_chunk(NC - 2, 0)
            c_chunk(NC - 1, 1)


def kernel(L0_attn_x, L0_attn_Wqk, L0_attn_bqk, L0_attn_Wv, L0_attn_bv, L0_attn_Wu, L0_attn_bu, L0_attn_Wo,
           L0_attn_bo, L0_attn_ln_g, L0_attn_ln_b, L0_ffn_w_gate, L0_ffn_w_up, L0_ffn_w_down):
    import concourse.bacc as bacc
    from concourse.bass_utils import run_bass_kernel_spmd

    x = np.asarray(L0_attn_x)
    _, n, d = x.shape
    nk, nc_ = d // P, L0_ffn_w_gate.shape[0] // P

    def by_group(v):
        return np.ascontiguousarray(np.asarray(v).reshape(nk, P).T)

    def rows(w):
        return np.ascontiguousarray(np.asarray(w).reshape(nk, P, -1))

    def chunks_in(w):
        w = np.asarray(w).reshape(nc_, P, nk, P)
        return np.ascontiguousarray(w.transpose(0, 3, 2, 1)).reshape(nc_, P, nk * P)

    arrays = {
        "x": np.ascontiguousarray(x[0]),
        "xT": np.ascontiguousarray(x[0].T.reshape(nk, P, n).transpose(1, 0, 2)),
        "wqk": rows(L0_attn_Wqk), "wv": rows(L0_attn_Wv), "wu": rows(L0_attn_Wu), "wo": rows(L0_attn_Wo),
        "wg": chunks_in(L0_ffn_w_gate), "wup": chunks_in(L0_ffn_w_up),
        "wd": np.ascontiguousarray(np.asarray(L0_ffn_w_down).T).reshape(nc_, P, d),
        "bqk": by_group(L0_attn_bqk), "bu": by_group(L0_attn_bu), "bo": by_group(L0_attn_bo),
        "ln_g": by_group(L0_attn_ln_g), "ln_b": by_group(L0_attn_ln_b),
        "bv": np.ascontiguousarray(np.asarray(L0_attn_bv)),
    }
    nc = bacc.Bacc("TRN2", target_bir_lowering=False, num_devices=1)
    args = {name: nc.dram_tensor(f"in_{name}", a.shape, mybir.dt.from_np(a.dtype), kind="ExternalInput").ap()
            for name, a in arrays.items()}
    outT = nc.dram_tensor("outT", (P, nk, n), F32, kind="ExternalOutput").ap()
    build(nc, **args, outT=outT)
    r = run_bass_kernel_spmd(nc, [{f"in_{name}": a for name, a in arrays.items()}], core_ids=[0])
    got = r.results[0]["outT"]
    return np.ascontiguousarray(got.transpose(2, 1, 0)).reshape(1, n, d)
```
